# Optimizing a Trainium2 kernel written in Bass

```python
import numpy as np
import jax
import jax.numpy as jnp

def _softmax(x, axis=-1):
    return jax.nn.softmax(x, axis=axis)

def _gelu(x):
    return jax.nn.gelu(x, approximate=True)

def _silu(x):
    return jax.nn.silu(x)

def _sigmoid(x):
    return jax.nn.sigmoid(x)

def _layernorm(x, axis=-1, eps=1e-05):
    m = jnp.mean(x, axis=axis, keepdims=True)
    v = jnp.var(x, axis=axis, keepdims=True)
    return (x - m) / jnp.sqrt(v + eps)

def _scatter_add(tgt, idx, src, axis=0):
    return tgt.at[idx].add(src)

def _segment_sum(src, seg, n):
    return jax.ops.segment_sum(src, seg, n)
kernel_name = 'mk_seq_preln_d2_jaxref_r8_d0d6a0'

def setup_inputs(seed: int=0):
    np.random.seed(seed)
    _w = jnp.asarray

    def _L0_attn_setup():
        import jax, jax.numpy as jnp
        import numpy as np
        B, N, DIM = (2, 256, 128)
        H = 16
        HD = DIM // H
        key = jax.random.key(seed)
        ks = jax.random.split(key, 4)
        x = jax.random.normal(ks[0], (B, N, DIM), dtype=jnp.float32)
        w_qkv = jax.random.normal(ks[1], (DIM, 3 * DIM), dtype=jnp.float32) / np.sqrt(DIM)
        w_proj = jax.random.normal(ks[2], (DIM, DIM), dtype=jnp.float32) / np.sqrt(DIM)
        b_proj = jax.random.normal(ks[3], (DIM,), dtype=jnp.float32) * 0.01
        return {'x': x, 'w_qkv': w_qkv, 'w_proj': w_proj, 'b_proj': b_proj}
    _L0_attn_in = _L0_attn_setup()

    def _L0_ffn_setup():
        import jax, jax.numpy as jnp
        import numpy as np
        BLOCK = 16
        _GRID = jnp.array([0.0, 0.5, 1.0, 1.5, 2.0, 3.0, 4.0, 6.0], dtype=jnp.float32)
        _MID = jnp.array([0.25, 0.75, 1.25, 1.75, 2.5, 3.5, 5.0], dtype=jnp.float32)

        def fp4_quant_dequant(x):
            shape = x.shape
            xb = x.reshape(shape[:-1] + (shape[-1] // BLOCK, BLOCK))
            scale = jnp.max(jnp.abs(xb), axis=-1, keepdims=True) / 6.0
            scale = jnp.maximum(scale, jnp.float32(1e-12))
            xn = xb / scale
            idx = jnp.searchsorted(_MID, jnp.abs(xn))
            q = _GRID[idx] * jnp.sign(xn) * scale
            return q.reshape(shape)

        def fp4_linear(x, w):
            xq = fp4_quant_dequant(x)
            wq = fp4_quant_dequant(w)
            return jnp.einsum('bsk,nk->bsn', xq, wq)
        key = jax.random.key(seed)
        k1, k2, k3, k4 = jax.random.split(key, 4)
        H, I = (128, 352)
        x = jax.random.normal(k1, (4, 512, H), dtype=jnp.float32)
        w_gate = jax.random.normal(k2, (I, H), dtype=jnp.float32) * 0.02
        w_up = jax.random.normal(k3, (I, H), dtype=jnp.float32) * 0.02
        w_down = jax.random.normal(k4, (H, I), dtype=jnp.float32) * 0.02
        return {'x': x, 'w_gate': w_gate, 'w_up': w_up, 'w_down': w_down}
    _L0_ffn_in = _L0_ffn_setup()

    def _L1_attn_setup():
        import jax, jax.numpy as jnp
        import numpy as np
        L, B, S, D, H, HID = (6, 4, 128, 128, 16, 512)
        HD = D // H

        def _pos_encoding(S, D):
            pos = np.arange(S)
            level = np.frexp((pos + 1).astype(np.float64))[1] - 1
            coord = (pos >> level) / 2.0 ** level
            div = np.exp(np.arange(0, D, 2, dtype=np.float64) * -(np.log(10000.0) / D))
            ang = pos[:, None].astype(np.float64) * div[None, :]
            pe = np.zeros((S, D), np.float32)
            pe[:, 0::2] = (np.sin(ang) * coord[:, None]).astype(np.float32)
            pe[:, 1::2] = (np.cos(ang) * coord[:, None]).astype(np.float32)
            return jnp.asarray(pe)

        def _sierpinski_mask(S):
            i = np.arange(S)
            return jnp.asarray((np.bitwise_and(i[:, None], i[None, :]) == 0).astype(np.float32))

        def _ln(h, g, b, eps=1e-05):
            m = h.mean(-1, keepdims=True)
            v = h.var(-1, keepdims=True)
            return (h - m) * jax.lax.rsqrt(v + eps) * g + b
        key = jax.random.key(seed)
        ks = iter(jax.random.split(key, 16))
        w = lambda k, shape: 0.02 * jax.random.normal(k, shape, jnp.float32)
        return {'x': jax.random.normal(next(ks), (B, S, D), jnp.float32), 'Wq': w(next(ks), (L, D, D)), 'bq': jnp.zeros((L, D), jnp.float32), 'Wk': w(next(ks), (L, D, D)), 'bk': jnp.zeros((L, D), jnp.float32), 'Wv': w(next(ks), (L, D, D)), 'bv': jnp.zeros((L, D), jnp.float32), 'Wo': w(next(ks), (L, D, D)), 'bo': jnp.zeros((L, D), jnp.float32), 'W1': w(next(ks), (L, D, HID)), 'b1': jnp.zeros((L, HID), jnp.float32), 'W2': w(next(ks), (L, HID, D)), 'b2': jnp.zeros((L, D), jnp.float32), 'ln1_g': jnp.ones((L, D), jnp.float32), 'ln1_b': jnp.zeros((L, D), jnp.float32), 'ln2_g': jnp.ones((L, D), jnp.float32), 'ln2_b': jnp.zeros((L, D), jnp.float32), 'lnf_g': jnp.ones((D,), jnp.float32), 'lnf_b': jnp.zeros((D,), jnp.float32)}
    _L1_attn_in = _L1_attn_setup()

    def _L1_ffn_setup():
        import jax, jax.numpy as jnp
        import numpy as np
        HIDDEN = 128
        INTER = 512
        key = jax.random.key(seed)
        k1, k2, k3, k4, k5 = jax.random.split(key, 5)
        hidden_states = jax.random.normal(k1, (4, 256, HIDDEN), dtype=jnp.float32)
        W1 = jax.random.normal(k2, (HIDDEN, INTER), dtype=jnp.float32) * (1.0 / np.sqrt(HIDDEN))
        b1 = jax.random.normal(k3, (INTER,), dtype=jnp.float32) * 0.02
        W2 = jax.random.normal(k4, (INTER, HIDDEN), dtype=jnp.float32) * (1.0 / np.sqrt(INTER))
        b2 = jax.random.normal(k5, (HIDDEN,), dtype=jnp.float32) * 0.02
        return {'hidden_states': hidden_states, 'W1': W1, 'b1': b1, 'W2': W2, 'b2': b2}
    _L1_ffn_in = _L1_ffn_setup()
    _d = {'L0_attn_x': _L0_attn_in['x'], 'L0_attn_w_qkv': _L0_attn_in['w_qkv'], 'L0_attn_w_proj': _L0_attn_in['w_proj'], 'L0_attn_b_proj': _L0_attn_in['b_proj'], 'L0_ffn_w_gate': _L0_ffn_in['w_gate'], 'L0_ffn_w_up': _L0_ffn_in['w_up'], 'L0_ffn_w_down': _L0_ffn_in['w_down'], 'L1_attn_Wq': _L1_attn_in['Wq'], 'L1_attn_bq': _L1_attn_in['bq'], 'L1_attn_Wk': _L1_attn_in['Wk'], 'L1_attn_bk': _L1_attn_in['bk'], 'L1_attn_Wv': _L1_attn_in['Wv'], 'L1_attn_bv': _L1_attn_in['bv'], 'L1_attn_Wo': _L1_attn_in['Wo'], 'L1_attn_bo': _L1_attn_in['bo'], 'L1_attn_W1': _L1_attn_in['W1'], 'L1_attn_b1': _L1_attn_in['b1'], 'L1_attn_W2': _L1_attn_in['W2'], 'L1_attn_b2': _L1_attn_in['b2'], 'L1_attn_ln1_g': _L1_attn_in['ln1_g'], 'L1_attn_ln1_b': _L1_attn_in['ln1_b'], 'L1_attn_ln2_g': _L1_attn_in['ln2_g'], 'L1_attn_ln2_b': _L1_attn_in['ln2_b'], 'L1_attn_lnf_g': _L1_attn_in['lnf_g'], 'L1_attn_lnf_b': _L1_attn_in['lnf_b'], 'L1_ffn_W1': _L1_ffn_in['W1'], 'L1_ffn_b1': _L1_ffn_in['b1'], 'L1_ffn_W2': _L1_ffn_in['W2'], 'L1_ffn_b2': _L1_ffn_in['b2']}
    _x0 = _d['L0_attn_x']
    _d['L0_attn_x'] = jax.random.normal(jax.random.fold_in(jax.random.key(seed), 1), (2, 1024, 128), dtype=_x0.dtype)
    del _x0
    return _d

def reference(L0_attn_x, L0_attn_w_qkv, L0_attn_w_proj, L0_attn_b_proj, L0_ffn_w_gate, L0_ffn_w_up, L0_ffn_w_down, L1_attn_Wq, L1_attn_bq, L1_attn_Wk, L1_attn_bk, L1_attn_Wv, L1_attn_bv, L1_attn_Wo, L1_attn_bo, L1_attn_W1, L1_attn_b1, L1_attn_W2, L1_attn_b2, L1_attn_ln1_g, L1_attn_ln1_b, L1_attn_ln2_g, L1_attn_ln2_b, L1_attn_lnf_g, L1_attn_lnf_b, L1_ffn_W1, L1_ffn_b1, L1_ffn_W2, L1_ffn_b2):

    def _L0_attn_ref(x, w_qkv, w_proj, b_proj):
        import jax, jax.numpy as jnp
        import numpy as np
        B, N, DIM = (2, 256, 128)
        H = 16
        HD = DIM // H
        b, n, c = x.shape
        scale = HD ** (-0.5)
        qkv = jnp.einsum('bnc,cd->bnd', x, w_qkv)
        qkv = qkv.reshape(b, n, 3, H, HD).transpose(2, 0, 3, 1, 4)
        q, k, v = (qkv[0], qkv[1], qkv[2])
        q = q * scale
        attn = jnp.einsum('bhnd,bhmd->bhnm', q, k)
        attn = jax.nn.softmax(attn, axis=-1)
        out = jnp.einsum('bhnm,bhmd->bhnd', attn, v)
        out = out.transpose(0, 2, 1, 3).reshape(b, n, c)
        return jnp.einsum('bnc,cd->bnd', out, w_proj) + b_proj

    def _L0_ffn_ref(x, w_gate, w_up, w_down):
        import jax, jax.numpy as jnp
        import numpy as np
        BLOCK = 16
        _GRID = jnp.array([0.0, 0.5, 1.0, 1.5, 2.0, 3.0, 4.0, 6.0], dtype=jnp.float32)
        _MID = jnp.array([0.25, 0.75, 1.25, 1.75, 2.5, 3.5, 5.0], dtype=jnp.float32)

        def fp4_quant_dequant(x):
            shape = x.shape
            xb = x.reshape(shape[:-1] + (shape[-1] // BLOCK, BLOCK))
            scale = jnp.max(jnp.abs(xb), axis=-1, keepdims=True) / 6.0
            scale = jnp.maximum(scale, jnp.float32(1e-12))
            xn = xb / scale
            idx = jnp.searchsorted(_MID, jnp.abs(xn))
            q = _GRID[idx] * jnp.sign(xn) * scale
            return q.reshape(shape)

        def fp4_linear(x, w):
            xq = fp4_quant_dequant(x)
            wq = fp4_quant_dequant(w)
            return jnp.einsum('bsk,nk->bsn', xq, wq)
        gate = fp4_linear(x, w_gate)
        y = fp4_linear(x, w_up)
        h = jax.nn.silu(gate) * y
        return fp4_linear(h, w_down)

    def _L1_attn_ref(x, Wq, bq, Wk, bk, Wv, bv, Wo, bo, W1, b1, W2, b2, ln1_g, ln1_b, ln2_g, ln2_b, lnf_g, lnf_b):
        import jax, jax.numpy as jnp
        import numpy as np
        L, B, S, D, H, HID = (6, 4, 128, 128, 16, 512)
        HD = D // H

        def _pos_encoding(S, D):
            pos = np.arange(S)
            level = np.frexp((pos + 1).astype(np.float64))[1] - 1
            coord = (pos >> level) / 2.0 ** level
            div = np.exp(np.arange(0, D, 2, dtype=np.float64) * -(np.log(10000.0) / D))
            ang = pos[:, None].astype(np.float64) * div[None, :]
            pe = np.zeros((S, D), np.float32)
            pe[:, 0::2] = (np.sin(ang) * coord[:, None]).astype(np.float32)
            pe[:, 1::2] = (np.cos(ang) * coord[:, None]).astype(np.float32)
            return jnp.asarray(pe)

        def _sierpinski_mask(S):
            i = np.arange(S)
            return jnp.asarray((np.bitwise_and(i[:, None], i[None, :]) == 0).astype(np.float32))

        def _ln(h, g, b, eps=1e-05):
            m = h.mean(-1, keepdims=True)
            v = h.var(-1, keepdims=True)
            return (h - m) * jax.lax.rsqrt(v + eps) * g + b
        Bx, Sx, Dx = x.shape
        smask = _sierpinski_mask(Sx)
        h = x + _pos_encoding(Sx, Dx)
        scale = 1.0 / jnp.sqrt(jnp.float32(HD))

        def layer(h, p):
            wq, bq_, wk, bk_, wv, bv_, wo, bo_, w1, b1_, w2, b2_, g1, be1, g2, be2 = p
            q = (h @ wq + bq_).reshape(Bx, Sx, H, HD).transpose(0, 2, 1, 3)
            k = (h @ wk + bk_).reshape(Bx, Sx, H, HD).transpose(0, 2, 1, 3)
            v = (h @ wv + bv_).reshape(Bx, Sx, H, HD).transpose(0, 2, 1, 3)
            scores = jnp.einsum('bhqd,bhkd->bhqk', q, k) * scale
            scores = scores * smask
            a = jax.nn.softmax(scores, axis=-1)
            att = jnp.einsum('bhqk,bhkd->bhqd', a, v)
            att = att.transpose(0, 2, 1, 3).reshape(Bx, Sx, Dx) @ wo + bo_
            h = _ln(h + att, g1, be1)
            ff = jax.nn.gelu(h @ w1 + b1_, approximate=False) @ w2 + b2_
            h = _ln(h + ff, g2, be2)
            return (h, None)
        params = (Wq, bq, Wk, bk, Wv, bv, Wo, bo, W1, b1, W2, b2, ln1_g, ln1_b, ln2_g, ln2_b)
        h, _ = jax.lax.scan(layer, h, params)
        return _ln(h, lnf_g, lnf_b)

    def _L1_ffn_ref(hidden_states, W1, b1, W2, b2):
        import jax, jax.numpy as jnp
        import numpy as np
        HIDDEN = 128
        INTER = 512
        h = jax.nn.relu(jnp.einsum('bsh,hi->bsi', hidden_states, W1) + b1)
        return jnp.einsum('bsi,ih->bsh', h, W2) + b2
    x = L0_attn_x
    x = x + _L0_attn_ref(_layernorm(x, axis=-1), L0_attn_w_qkv, L0_attn_w_proj, L0_attn_b_proj)
    x = x + _L0_ffn_ref(_layernorm(x, axis=-1), L0_ffn_w_gate, L0_ffn_w_up, L0_ffn_w_down)
    x = x + _L1_attn_ref(_layernorm(x, axis=-1), L1_attn_Wq, L1_attn_bq, L1_attn_Wk, L1_attn_bk, L1_attn_Wv, L1_attn_bv, L1_attn_Wo, L1_attn_bo, L1_attn_W1, L1_attn_b1, L1_attn_W2, L1_attn_b2, L1_attn_ln1_g, L1_attn_ln1_b, L1_attn_ln2_g, L1_attn_ln2_b, L1_attn_lnf_g, L1_attn_lnf_b)
    x = x + _L1_ffn_ref(_layernorm(x, axis=-1), L1_ffn_W1, L1_ffn_b1, L1_ffn_W2, L1_ffn_b2)
    return x

_drawn_inputs = setup_inputs


def setup_inputs(seed=0):
    import zlib

    import numpy as np

    out = dict(_drawn_inputs(seed))
    spreads = {'L1_attn_bq': (0.0, 0.8),
     'L1_attn_bk': (0.0, 2.0),
     'L1_attn_bv': (0.0, 0.283),
     'L1_attn_bo': (0.0, 0.1),
     'L1_attn_b1': (0.0, 0.405),
     'L1_attn_b2': (0.0, 0.1),
     'L1_attn_ln1_g': (1.0, 0.2),
     'L1_attn_ln1_b': (0.0, 0.1),
     'L1_attn_ln2_g': (1.0, 0.2),
     'L1_attn_ln2_b': (0.0, 0.1),
     'L1_attn_lnf_g': (1.0, 0.2),
     'L1_attn_lnf_b': (0.0, 0.1)}
    factors = {'L0_attn_b_proj': 6.051,
     'L0_ffn_w_gate': 5.667,
     'L0_ffn_w_up': 5.434,
     'L0_ffn_w_down': 5.432,
     'L1_attn_Wq': 8.0,
     'L1_attn_Wk': 8.0,
     'L1_attn_Wv': 2.981,
     'L1_ffn_b1': 8.0,
     'L1_ffn_b2': 5.592}
    for name, (base, spread) in spreads.items():
        noise = np.random.default_rng([zlib.crc32(name.encode()), seed]).standard_normal(out[name].shape)
        drawn = base * np.exp(spread * noise) if base else spread * noise
        out[name] = jnp.asarray(drawn.astype(out[name].dtype))
    for name, factor in factors.items():
        out[name] = (out[name] * factor).astype(out[name].dtype)
    return out
```

```python
from contextlib import ExitStack

import concourse.bass as bass
from concourse import mybir

F32 = mybir.dt.float32
BF16 = mybir.dt.bfloat16
I32 = mybir.dt.int32
ACT = mybir.ActivationFunctionType
ALU = mybir.AluOpType
AX = mybir.AxisListType

P = 128
D = 128
B, S = 2, 1024
H, HD = 16, 8
NB = S // P
NT = B * NB
CH = 512
TC = CH // P
NC = NT // TC
HG = 4
NG = H // HG
U = B * NG
VW = HD + 1
VT = H * VW
NP = 3
R_PAIR = NP * NP * HD
NBIT = 10
R_A = R_PAIR + NBIT
R_B = R_A + NP
RING = 4
PBUF = 3
LAG = 2
LAYERS = 6
HID = 512
NHID = HID // P
FF0 = 352
QB = 16
EPS = 1e-5
SCALE = float(HD) ** -0.5
GRID_UP = (5.0, 3.5, 2.5)
GRID_LOW = (0.25, 0.75, 1.25, 1.75)


def groups_of(sparse):
    groups, bundles = [], []
    for r in range(NB):
        halves = [0, 1] if (r == 0 or not sparse) else [None]
        for half in halves:
            width = CH if half is not None else P * (1 << (3 - bin(r).count("1")))
            per = CH // width
            first = len(groups)
            for h in range(0, HG, per):
                groups.append((r, half, list(range(h, h + per)), width))
            bundles.append((r, half, width, first, len(groups) - first))
    return groups, bundles


def blocks(ap, r, half):
    if half is not None:
        return ap[:, half * CH:(half + 1) * CH]
    v = ap.rearrange("p (a b c t) -> p a b c t", a=2, b=2, c=2)
    return {1: lambda: v[:, :, :, 0, :], 2: lambda: v[:, :, 0, :, :], 4: lambda: v[:, 0, :, :, :],
            3: lambda: v[:, :, 0, 0, :], 5: lambda: v[:, 0, :, 0, :], 6: lambda: v[:, 0, 0, :, :],
            7: lambda: v[:, 0, 0, 0, :]}[r]()


def out_parts(r, half, width):
    if half is not None:
        return [(half, 0, width)]
    if r & 4:
        return [(0, 0, width)]
    return [(0, 0, width // 2), (1, width // 2, width // 2)]


def bank_cols(ap, r, half):
    if half is not None:
        return ap
    v = ap.rearrange("p (b c t) -> p b c t", b=2, c=2)
    return {0: lambda: v, 1: lambda: v[:, :, 0, :], 2: lambda: v[:, 0, :, :],
            3: lambda: v[:, 0, 0, :]}[r & 3]()


class Attn:

    def __init__(self, sem, tag, sparse, delay):
        self.sparse = sparse
        self.groups, self.bundles = groups_of(sparse)
        self.n = len(self.groups)
        self.nb = len(self.bundles)
        self.lead = self.n + delay
        self.steps = U * self.n + self.lead + LAG + 8
        self.bundle_of = {}
        for k, (_, _, _, first, cnt) in enumerate(self.bundles):
            for g in range(first, first + cnt):
                self.bundle_of[g] = (k, g - first)

        def s(name):
            return sem(f"{tag}_{name}")

        self.ht_filled, self.ht_ready = s("ht_filled"), s("ht_ready")
        self.qk_filled, self.qk_evac = s("qk_filled"), s("qk_evac")
        self.qk_res, self.qk_mid, self.qk_split = s("qk_res"), s("qk_mid"), s("qk_split")
        self.q_written, self.k_written = s("q_written"), s("k_written")
        self.stack = [s(f"stack{i}") for i in range(RING)]
        self.v_filled, self.v_evac = s("v_filled"), s("v_evac")
        self.a_scored, self.a_reduced = s("a_scored"), s("a_reduced")
        self.mx = s("mx")
        self.mt_filled, self.mt_evac = s("mt_filled"), s("mt_evac")
        self.m_written, self.m_loaded = s("m_written"), s("m_loaded")
        self.b_scored, self.b_exped = s("b_scored"), s("b_exped")
        self.av_done = s("av_done")
        self.o_evac = s("o_evac")
        self.ot_filled, self.ot_read = s("ot_filled"), s("ot_read")
        self.rec, self.at_ready = s("rec"), s("at_ready")
        self.aht_filled, self.aht_ready = s("aht_filled"), s("aht_ready")
        self.wo_filled, self.res = s("wo_filled"), s("res")
        self.hb_step = s("hb_step")
        if not sparse:
            return
        self.bqs = s("bqs")
        self.em_ready = s("em_ready")
        self.u_step = s("u_step")
        self.vm_filled, self.vm_scaled, self.vm_added = s("vm_filled"), s("vm_scaled"), s("vm_added")


MXN = 6


def build(nc, io):
    ctx = ExitStack()
    with ctx:
        def sb(name, shape, dt=F32):
            return ctx.enter_context(nc.sbuf_tensor(name, shape, dt))

        def sem(name):
            return ctx.enter_context(nc.semaphore(name))

        def wait(eng, s, n, layer=0, per=0):
            if n > 0:
                eng.wait_ge(s, n if isinstance(layer, int) else layer * per + n)

        X = sb("X", [P, NT, D])
        N = sb("N", [P, NT, D])
        HB = sb("HB", [P, NT, D])
        HT = sb("HT", [P, NT * P])
        QS = sb("QS", [P, RING, HG, S], BF16)
        KS = sb("KS", [P, RING, HG, S], BF16)
        V = sb("V", [P, NT * VT + 32])
        VU = sb("VU", [P, B, NB, VT])
        PB = sb("PB", [P, PBUF, HG * CH])
        OT = sb("OT", [P, S])
        ON = sb("ON", [P, NT, H, VW])
        PQ = sb("PQ", [P, NP, S], BF16)
        PK = sb("PK", [P, NP, S], BF16)
        ident = sb("ident", [P, P])
        identb = sb("identb", [P, P], BF16)
        ones = sb("ones", [P, P])
        negm = sb("negm", [P, P])
        floors = sb("floors", [P, 2, NB])
        pos = HT[:, NB * D:2 * NB * D].rearrange("p (t d) -> p t d", d=D)
        wE = sb("wE", [P, 3, D])
        cE = sb("cE", [P, 4])
        rE = sb("rE", [P, 4, D])
        wL = sb("wL", [P, D + 2 * HID])
        cL = sb("cL", [P, 2 + NHID])
        rL = sb("rL", [P, 3, D])
        bqs = sb("bqs", [P, 1])
        mx = sb("mx", [P, 2, HG, NB])
        mxb = sb("mxb", [P, 2, HG, NB])
        mres = sb("mres", [P, HG, NB])
        mp = sb("mp", [P, NP, HG, NB], BF16)
        mt = sb("mt", [NP * HG * NB, P], BF16)
        emx = sb("emx", [P, 2, HG, NB])
        em = sb("em", [P, B, NG, HG, NB])
        rec = sb("rec", [P, NT, H])
        bst = sb("bst", [P, 2, TC, 6])
        mv = sb("mv", [P, NT, 2])
        vareps = sb("vareps", [P, NT])
        rstd = sb("rstd", [P, NT])
        mhalf = sb("mhalf", [P, NT])
        rider = sb("rider", [P, 2 * NC])
        vmt = OT[:, 0:3 * VT]
        x32 = PB[:, 2, 0:2 * CH].rearrange("p (k t) -> p k t", k=2)
        FF = PB[:, 0:2, :].rearrange("p k (m t) -> p k m t", m=NHID)

        def psum(name):
            return ctx.enter_context(nc.psum_tensor(name, [P, 2, CH], F32))

        pA, pB, pO, pG = psum("pA"), psum("pB"), psum("pO"), psum("pG")

        scq = nc.dram_tensor("scq", (B, NP, NP, P, S), BF16, kind="Internal").ap()
        sck = nc.dram_tensor("sck", (B, NP, P, S), BF16, kind="Internal").ap()
        scm = nc.dram_tensor("scm", (U, NP, HG * S), BF16, kind="Internal").ap()

        A0 = Attn(sem, "a0", False, 12)
        A1 = Attn(sem, "a1", True, 10)

        x_in = sem("x_in")
        consts_in = sem("consts_in")
        made = sem("made")
        mask_in = sem("mask_in")
        wE_in, wL_in = sem("wE_in"), sem("wL_in")

        class LN:

            def __init__(self, sems, before=0):
                self.st, self.ag, self.ve, self.rs, self.ready = sems
                self.off = before * NC

        def ln_sems(tag):
            return [sem(f"{tag}_{k}") for k in ("stats", "aggr", "vareps", "rstd", "ready")]

        ln_outer = ln_sems("ln")
        lnA, lnB, lnC, lnF, lnD = (LN(ln_outer, k) for k in range(5))
        ln1, ln2 = LN(ln_sems("ln1")), LN(ln_sems("ln2"))

        def ln_stats(v, ln, src, c, layer=0, wait_col=0):
            for i in range(TC):
                ins = v.bn_stats(bst[:, c % 2, i, :], src[:, TC * c + i, :])
            ins.then_inc(ln.st, 1)
            wait(v, ln.st, ln.off + c + 1, layer, NC)
            if not isinstance(layer, int):
                v.memset(rider[:, wait_col + c:wait_col + c + 1], 0.0)
            for i in range(TC):
                ins = v.bn_aggr(mv[:, TC * c + i, :], bst[:, c % 2, i, :])
            ins.then_inc(ln.ag, 1)
            wait(v, ln.ag, ln.off + c + 1, layer, NC)
            v.tensor_scalar(vareps[:, TC * c:TC * c + TC], mv[:, TC * c:TC * c + TC, 1], EPS, None,
                            ALU.add).then_inc(ln.ve, 1)

        def ln_norm(v, ln, src, dst, c, layer=0):
            wait(v, ln.rs, ln.off + c + 1, layer, NC)
            for i in range(TC):
                t = TC * c + i
                ins = v.tensor_scalar(dst[:, t, :], src[:, t, :], mv[:, t, 0:1], rstd[:, t:t + 1],
                                      ALU.subtract, ALU.mult)
            ins.then_inc(ln.ready, 1)

        def ln_pow(g, ln, c, layer=0):
            wait(g, ln.ve, ln.off + c + 1, layer, NC)
            a = slice(TC * c, TC * c + TC)
            g.tensor_tensor(rstd[:, a], vareps[:, a], mhalf[:, a], ALU.pow).then_inc(ln.rs, 1)

        def transposes(pe, src, c):
            for i in range(TC):
                ins = pe.transpose(pG[:, c % 2, i * P:(i + 1) * P], src[:, TC * c + i, :], ident[:, :])
            return ins

        def pe_project(pe, a, ready, layer, wq, wk, wv, per_ready=NC):
            for c in range(NC):
                wait(pe, ready, c + 1, layer, per_ready)
                wait(pe, a.ht_ready, c - 1, layer, NC)
                transposes(pe, N, c).then_inc(a.ht_filled, 1)
            wait(pe, a.ht_ready, NC, layer, NC)
            for c in range(NC):
                for k, w in enumerate((wq, wk)):
                    z = 2 * c + k
                    wait(pe, a.qk_evac, z - 1, layer, 2 * NC)
                    pe.matmul(pG[:, z % 2, :], w, HT[:, c * CH:(c + 1) * CH], start=True, stop=True)\
                        .then_inc(a.qk_filled, 1)
            for c in range(NC):
                wait(pe, a.qk_evac, min(2 * NC, 2 * NC - 1 + c), layer, 2 * NC)
                wait(pe, a.v_evac, c - 1, layer, NC)
                for i in range(TC):
                    t = TC * c + i
                    ins = pe.matmul(pG[:, c % 2, i * P:(i + 1) * P], HT[:, t * P:(t + 1) * P], wv,
                                    start=True, stop=True)
                ins.then_inc(a.v_filled, 1)

        def pe_attend(pe, a, layer):
            for t in range(a.steps):
                s, n = divmod(t, a.n)
                if s < U:
                    r, half, heads, width = a.groups[n]
                    if n == 0:
                        wait(pe, a.stack[s % RING], 64 * (s // RING + 1), layer, 64 * U // RING)
                    wait(pe, a.a_reduced, t - 1, layer, U * a.n)
                    for k, h in enumerate(heads):
                        out = pA[:, t % 2, k * width:(k + 1) * width]
                        ins = pe.matmul(out, QS[0:R_A, s % RING, h, r * P:(r + 1) * P],
                                        blocks(KS[0:R_A, s % RING, h, :], r, half), start=True, stop=True)
                    ins.then_inc(a.a_scored, 1)
                s, n = divmod(t - 1, a.n)
                if n == 0 and 1 <= s <= U:
                    s -= 1
                    wait(pe, a.mx, MXN * (s + 1), layer, MXN * U)
                    wait(pe, a.v_evac, NC, layer, NC)
                    wait(pe, a.ot_read, 2 * max(0, s - 2), layer, 2 * U)
                    pe.transpose(pG[:, 0, :].bitcast(BF16)[0:NP * HG * NB, 0:P],
                                 mp[:, :, :, :].rearrange("p a b c -> p (a b c)"), identb[:, :])\
                        .then_inc(a.mt_filled, 1)
                t_b = t - a.lead
                s, n = divmod(t_b, a.n)
                if 0 <= s < U:
                    r, half, heads, width = a.groups[n]
                    if n == 0:
                        wait(pe, a.m_loaded, 16 * (s + 1), layer, 16 * U)
                    wait(pe, a.b_exped, t_b - 1, layer, U * a.n)
                    for k, h in enumerate(heads):
                        out = pB[:, t_b % 2, k * width:(k + 1) * width]
                        ins = pe.matmul(out, KS[0:R_B, s % RING, h, r * P:(r + 1) * P],
                                        blocks(QS[0:R_B, s % RING, h, :], r, half), start=True, stop=True)
                    ins.then_inc(a.b_scored, 1)
                t_v = t_b - LAG
                s, n = divmod(t_v, a.n)
                if 0 <= s < U:
                    k, _ = a.bundle_of[n]
                    r, half, width, first, cnt = a.bundles[k]
                    if n == first + cnt - 1:
                        wait(pe, a.b_exped, t_v + 1, layer, U * a.n)
                        if k == 0:
                            wait(pe, a.o_evac, s, layer, U)
                        tile = (s // NG) * NB + r
                        for bank, off, w in out_parts(r, half, width):
                            for h in range(HG):
                                col = tile * VT + ((s % NG) * HG + h) * VW
                                at = h * width + off
                                ins = pe.matmul(
                                    bank_cols(pO[32 * h:32 * h + 32, bank, :], r, half),
                                    V[:, col:col + 32], PB[:, (s * a.nb + k) % PBUF, at:at + w],
                                    start=(r == 0), stop=(r == NB - 1), tile_position=(0, 32 * h),
                                    skip_group_check=True)
                        ins.then_inc(a.av_done, 1)
                s, n = divmod(t_v - 4, a.n)
                if n == 0 and 1 <= s <= U:
                    s -= 1
                    wait(pe, a.o_evac, s + 1, layer, U)
                    wait(pe, a.mt_evac, min(U, s + 2), layer, U)
                    for k in range(2):
                        wait(pe, a.ot_read, 2 * s, layer, 2 * U)
                        for i in range(TC):
                            j = TC * k + i
                            ins = pe.transpose(pG[:, k, i * P:(i + 1) * P], OT[:, j * P:(j + 1) * P],
                                               ident[:, :])
                        ins.then_inc(a.ot_filled, 1)

        VM_TILES = [(b, i0, min(3, NB - i0)) for b in range(B) for i0 in range(0, NB, 3)]

        def pe_masked(pe, a, layer):
            wait(pe, a.u_step, 4 * B, layer, 4 * B)
            for z, (b, i0, cnt) in enumerate(VM_TILES):
                wait(pe, a.ot_read, 2 * U, layer, 2 * U)
                wait(pe, a.vm_scaled, z - 1, layer, len(VM_TILES))
                for k in range(cnt):
                    out = pG[:, z % 2, k * VT:(k + 1) * VT]
                    pe.matmul(out, ones[:, :], VU[:, b, NB - 1, :], start=True, stop=False)
                    ins = pe.matmul(out, negm[:, :], VU[:, b, NB - 1 - i0 - k, :], start=False, stop=True)
                ins.then_inc(a.vm_filled, 1)

        def pe_output(pe, a, layer, wo):
            for c in range(NC):
                wait(pe, a.at_ready, c + 1, layer, NC)
                wait(pe, a.aht_ready, c - 1, layer, NC)
                transposes(pe, N, c).then_inc(a.aht_filled, 1)
            wait(pe, a.aht_ready, NC, layer, NC)
            for c in range(NC):
                wait(pe, a.res, c - 1, layer, NC)
                for i in range(TC):
                    t = TC * c + i
                    ins = pe.matmul(pG[:, c % 2, i * P:(i + 1) * P], HT[:, t * P:(t + 1) * P], wo,
                                    start=True, stop=True)
                ins.then_inc(a.wo_filled, 1)

        def act_project(act, a, layer, scale_col, bias_col, ready_in=None):
            for c in range(NC):
                wait(act, a.ht_filled, c + 1, layer, NC)
                act.activation(HT[:, c * CH:(c + 1) * CH], pG[:, c % 2, :], ACT.Identity,
                               scale=scale_col, bias=bias_col).then_inc(a.ht_ready, 1)
            if a.sparse:
                wait(act, a.bqs, 1, layer, 1)
            for c in range(NC):
                for k in range(2):
                    z = 2 * c + k
                    wait(act, a.qk_filled, z + 1, layer, 2 * NC)
                    wait(act, a.qk_split, z - 1, layer, 2 * NC)
                    if c >= 2:
                        wait(act, (a.q_written, a.k_written)[k], (48, 16)[k], layer, (48 * B, 16 * B)[k])
                    scale = SCALE if k == 0 else 1.0
                    bias = (bqs[:, 0:1] if k == 0 else cE[:, 1:2]) if a.sparse else 0.0
                    act.activation(x32[:, k, :], pG[:, z % 2, :], ACT.Identity, scale=scale, bias=bias)
                    act.activation((PQ, PK)[k][:, 0, (c % 2) * CH:(c % 2 + 1) * CH], pG[:, z % 2, :],
                                   ACT.Identity, scale=scale, bias=bias).then_inc(a.qk_evac, 1)

        def act_attend(act, a, layer):
            for t in range(a.steps):
                s, n = divmod(t - 1, a.n)
                if n == 0 and 1 <= s <= U:
                    s -= 1
                    wait(act, a.mt_filled, s + 1, layer, U)
                    wait(act, a.m_written, 16 * s, layer, 16 * U)
                    act.activation(mt[:, :], pG[:, 0, :].bitcast(BF16)[0:NP * HG * NB, 0:P], ACT.Copy)\
                        .then_inc(a.mt_evac, 1)
                    if a.sparse:
                        wait(act, a.mx, MXN * (s + 1), layer, MXN * U)
                        act.activation(em[:, s // NG, s % NG, :, :], emx[:, s % 2, :, :], ACT.Exp,
                                       scale=-1.0).then_inc(a.em_ready, 1)
                t_b = t - a.lead
                s, n = divmod(t_b, a.n)
                if 0 <= s < U:
                    k, at = a.bundle_of[n]
                    kb = s * a.nb + k
                    wait(act, a.b_scored, t_b + 1, layer, U * a.n)
                    if at == 0:
                        wait(act, a.av_done, kb - PBUF + 1, layer, U * a.nb)
                    act.activation(PB[:, kb % PBUF, at * CH:(at + 1) * CH], pB[:, t_b % 2, :], ACT.Exp)\
                        .then_inc(a.b_exped, 1)
                s, n = divmod(t_b - LAG, a.n)
                if n == 0 and 1 <= s <= U:
                    s -= 1
                    wait(act, a.av_done, (s + 1) * a.nb, layer, U * a.nb)
                    wait(act, a.ot_filled, 2 * s, layer, 2 * U)
                    act.activation(OT[:, :], pO[:, :, :].rearrange("p a b -> p (a b)"), ACT.Identity)\
                        .then_inc(a.o_evac, 1)

        def act_output(act, a, layer):
            for c in range(NC):
                wait(act, a.aht_filled, c + 1, layer, NC)
                act.activation(HT[:, c * CH:(c + 1) * CH], pG[:, c % 2, :], ACT.Identity)\
                    .then_inc(a.aht_ready, 1)

        def dve_project(v, a, layer, bv):
            for c in range(NC):
                for k in range(2):
                    z = 2 * c + k
                    hi, mid, lo = ((PQ, PK)[k][:, j, (c % 2) * CH:(c % 2 + 1) * CH] for j in range(NP))
                    wait(v, a.qk_evac, z + 1, layer, 2 * NC)
                    v.tensor_tensor(x32[:, k, :], x32[:, k, :], hi, ALU.subtract).then_inc(a.qk_res, 1)
                    wait(v, a.qk_res, z + 1, layer, 2 * NC)
                    v.tensor_copy(mid, x32[:, k, :]).then_inc(a.qk_mid, 1)
                    wait(v, a.qk_mid, z + 1, layer, 2 * NC)
                    v.tensor_tensor(lo, x32[:, k, :], mid, ALU.subtract).then_inc(a.qk_split, 1)
            for c in range(NC):
                wait(v, a.v_filled, c + 1, layer, NC)
                out = V[:, TC * c * VT:TC * (c + 1) * VT].rearrange("p (t h w) -> p t h w", t=TC, w=VW)
                src = pG[:, c % 2, :].rearrange("p (t h w) -> p t h w", t=TC, w=HD)
                if bv is None:
                    ins = v.tensor_copy(out[:, :, :, 0:HD], src)
                else:
                    row = bv.rearrange("p (h w) -> p h w", w=HD).unsqueeze(1).to_broadcast([P, TC, H, HD])
                    ins = v.tensor_tensor(out[:, :, :, 0:HD], src, row, ALU.add)
                ins.then_inc(a.v_evac, 1)

        def dve_attend(v, a, layer):
            for t in range(a.steps):
                s, n = divmod(t, a.n)
                if s < U:
                    r, half, heads, width = a.groups[n]
                    wait(v, a.a_scored, t + 1, layer, U * a.n)
                    if n == 0:
                        wait(v, a.mx, MXN * (s - 1), layer, MXN * U)
                        if a.sparse:
                            wait(v, a.em_ready, s - 1, layer, U)
                    dst = (mxb if half == 1 else mx)[:, s % 2, heads[0]:heads[-1] + 1, r]
                    v.tensor_reduce(dst, pA[:, t % 2, :].rearrange("p (h w) -> p h w", w=width), AX.X, ALU.max)\
                        .then_inc(a.a_reduced, 1)
                    if n == a.n - 1:
                        m, e = mx[:, s % 2, :, :], emx[:, s % 2, :, :]
                        base = MXN * s
                        wait(v, a.a_reduced, t + 1, layer, U * a.n)
                        if a.sparse:
                            v.tensor_tensor(m[:, :, 0], m[:, :, 0], mxb[:, s % 2, :, 0], ALU.max)\
                                .then_inc(a.mx, 1)
                        else:
                            v.tensor_tensor(m, m, mxb[:, s % 2, :, :], ALU.max).then_inc(a.mx, 1)
                        wait(v, a.mx, base + 1, layer, MXN * U)
                        if a.sparse:
                            v.tensor_tensor(e, m, floors[:, 1:2, :].to_broadcast([P, HG, NB]), ALU.max)
                            v.tensor_tensor(m, m, floors[:, 0:1, :].to_broadcast([P, HG, NB]), ALU.max)\
                                .then_inc(a.mx, 1)
                        else:
                            v.tensor_copy(e, m).then_inc(a.mx, 1)
                        wait(v, a.mx, base + 2, layer, MXN * U)
                        wait(v, a.mt_filled, s, layer, U)
                        v.tensor_scalar(mp[:, 0, :, :], m, -1.0, None, ALU.mult).then_inc(a.mx, 1)
                        wait(v, a.mx, base + 3, layer, MXN * U)
                        v.scalar_tensor_tensor(mres[:, :, :], m, -1.0, mp[:, 0, :, :], ALU.mult, ALU.subtract)\
                            .then_inc(a.mx, 1)
                        wait(v, a.mx, base + 4, layer, MXN * U)
                        v.tensor_copy(mp[:, 1, :, :], mres[:, :, :]).then_inc(a.mx, 1)
                        wait(v, a.mx, base + 5, layer, MXN * U)
                        v.tensor_tensor(mp[:, 2, :, :], mres[:, :, :], mp[:, 1, :, :], ALU.subtract)\
                            .then_inc(a.mx, 1)
                s, n = divmod(t - a.lead - LAG - 4, a.n)
                if n == 0 and 1 <= s <= U:
                    s -= 1
                    b, g = divmod(s, NG)
                    for k in range(2):
                        wait(v, a.ot_filled, 2 * s + k + 1, layer, 2 * U)
                        src = pG[:, k, :].rearrange("p (t h w) -> p t h w", t=TC, w=32)[:, :, :, 0:VW]
                        v.tensor_copy(ON[:, b * NB + TC * k:b * NB + TC * (k + 1), HG * g:HG * (g + 1), :], src)\
                            .then_inc(a.ot_read, 1)

        def dve_masked(v, a, layer):
            wait(v, a.em_ready, U, layer, U)
            for z, (b, i0, cnt) in enumerate(VM_TILES):
                on = ON[:, b * NB + i0:b * NB + i0 + cnt, :, :]
                scl = em[:, b, :, :, i0:i0 + cnt].rearrange("p g h i -> p i (g h)")\
                    .unsqueeze(3).to_broadcast([P, cnt, H, VW])
                tmp = vmt[:, 0:cnt * VT].rearrange("p (t h w) -> p t h w", t=cnt, w=VW)
                wait(v, a.vm_filled, z + 1, layer, len(VM_TILES))
                wait(v, a.vm_added, z, layer, len(VM_TILES))
                wait(v, a.ot_read, 2 * U, layer, 2 * U)
                v.tensor_tensor(tmp, pG[:, z % 2, 0:cnt * VT].rearrange("p (t h w) -> p t h w", t=cnt, w=VW),
                                scl, ALU.mult).then_inc(a.vm_scaled, 1)
                wait(v, a.vm_scaled, z + 1, layer, len(VM_TILES))
                v.tensor_tensor(on, on, tmp, ALU.add).then_inc(a.vm_added, 1)

        def dve_divide(v, a, layer):
            if a.sparse:
                wait(v, a.vm_added, len(VM_TILES), layer, len(VM_TILES))
                wait(v, a.hb_step, 3, layer, 3)
            else:
                wait(v, a.ot_read, 2 * U, layer, 2 * U)
            for c in range(NC):
                ts = slice(TC * c, TC * (c + 1))
                v.reciprocal(rec[:, ts, :], ON[:, ts, :, HD]).then_inc(a.rec, 1)
                wait(v, a.rec, c + 1, layer, NC)
                v.tensor_tensor(N[:, ts, :].rearrange("p t (h w) -> p t h w", w=HD), ON[:, ts, :, 0:HD],
                                rec[:, ts, :].unsqueeze(3).to_broadcast([P, TC, H, HD]), ALU.mult)\
                    .then_inc(a.at_ready, 1)

        def dve_residual(v, a, layer, dst, ln):
            for c in range(NC):
                ts = slice(TC * c, TC * (c + 1))
                wait(v, a.wo_filled, c + 1, layer, NC)
                wait(v, a.hb_step, 3, layer, 3)
                v.tensor_tensor(dst[:, ts, :], pG[:, c % 2, :].rearrange("p (t d) -> p t d", t=TC),
                                HB[:, ts, :], ALU.add).then_inc(a.res, 1)
                wait(v, a.res, c + 1, layer, NC)
                ln_stats(v, ln, dst, c, layer)
                if c:
                    ln_norm(v, ln, dst, N, c - 1, layer)
            ln_norm(v, ln, dst, N, NC - 1, layer)

        def load_stack(sp, a, s, layer):
            b, g = divmod(s, NG)
            if s >= RING:
                wait(sp, a.b_scored, (s - RING + 1) * a.n, layer, U * a.n)
            hs = slice(HG * g, HG * (g + 1))
            q = scq[b].rearrange("i j (d h) t -> (i j d) h t", h=H)
            k = sck[b].rearrange("j (d h) t -> (j d) h t", h=H)
            done = a.stack[s % RING]
            sp.dma_start(QS[0:R_PAIR, s % RING, :, :], q[:, hs, :]).then_inc(done, 16)
            for i in range(NP):
                sp.dma_start(KS[i * NP * HD:(i + 1) * NP * HD, s % RING, :, :], k[:, hs, :]).then_inc(done, 16)

        def sp_attend(sp, a, layer):
            for b in range(B):
                wait(sp, a.qk_split, 2 * NC // B * (b + 1), layer, 2 * NC)
                for j in range(NP):
                    sp.dma_start(scq[b, :, j].rearrange("i p t -> p i t"), PQ[:, :, :]).then_inc(a.q_written, 16)
                sp.dma_start(sck[b].rearrange("j p t -> p j t"), PK[:, :, :]).then_inc(a.k_written, 16)
                wait(sp, a.q_written, 48 * (b + 1), layer, 48 * B)
                wait(sp, a.k_written, 16 * (b + 1), layer, 16 * B)
                if b == 0:
                    for s in range(RING):
                        load_stack(sp, a, s, layer)
            for s in range(U):
                wait(sp, a.mt_evac, s + 1, layer, U)
                sp.dma_start(scm[s].rearrange("a (x t) -> (a x) t", t=P), mt[:, :]).then_inc(a.m_written, 16)
                wait(sp, a.m_written, 16 * (s + 1), layer, 16 * U)
                sp.dma_start(QS[R_A:R_B, s % RING, :, :].rearrange("p h t -> p (h t)"), scm[s])\
                    .then_inc(a.m_loaded, 16)
                if s >= 1 and s - 1 + RING < U:
                    load_stack(sp, a, s - 1 + RING, layer)

        FFN = []
        for c in range(NC + 1):
            if c < NC:
                FFN += [("hid", c, m) for m in range(NHID)]
            if c >= 1:
                FFN.append(("out", c - 1, 0))

        class Ffn:
            def __init__(self, tag):
                self.ht_filled, self.ht_ready = sem(f"{tag}_ht_filled"), sem(f"{tag}_ht_ready")
                self.filled = sem(f"{tag}_filled")
                self.hid = sem(f"{tag}_hid")
                self.out = sem(f"{tag}_out")

        def ffn_count(upto, kind):
            return sum(1 for u in FFN[:upto] if u[0] == kind)

        def pe_ffn(pe, f, ready, off, layer, w1, w2, before=None):
            for c in range(NC):
                if before is not None and c < 2:
                    wait(pe, before, NC - 1 + c, layer, NC)
                wait(pe, ready, off + c + 1, layer, NC)
                wait(pe, f.ht_ready, c - 1, layer, NC)
                transposes(pe, N, c).then_inc(f.ht_filled, 1)
            wait(pe, f.ht_ready, NC, layer, NC)
            for z, (kind, c, m) in enumerate(FFN):
                if z >= 2:
                    k2 = FFN[z - 2][0]
                    wait(pe, f.hid if k2 == "hid" else f.out, ffn_count(z - 1, k2), layer,
                         NC * NHID if k2 == "hid" else NC)
                if kind == "hid":
                    pe.matmul(pG[:, z % 2, :], w1[:, m * P:(m + 1) * P], HT[:, c * CH:(c + 1) * CH],
                              start=True, stop=True).then_inc(f.filled, 1)
                else:
                    wait(pe, f.hid, NHID * (c + 1), layer, NC * NHID)
                    for i in range(TC):
                        for k in range(NHID):
                            ins = pe.matmul(pG[:, z % 2, i * P:(i + 1) * P], FF[:, c % 2, k, i * P:(i + 1) * P],
                                            w2[:, k * D:(k + 1) * D], start=(k == 0), stop=(k == NHID - 1))
                    ins.then_inc(f.filled, 1)

        def act_ffn(act, f, layer, func, b1, scale_col=1.0, bias_col=0.0):
            for c in range(NC):
                wait(act, f.ht_filled, c + 1, layer, NC)
                act.activation(HT[:, c * CH:(c + 1) * CH], pG[:, c % 2, :], ACT.Identity,
                               scale=scale_col, bias=bias_col).then_inc(f.ht_ready, 1)
            for z, (kind, c, m) in enumerate(FFN):
                if kind == "hid":
                    wait(act, f.filled, z + 1, layer, len(FFN))
                    act.activation(FF[:, c % 2, m, :], pG[:, z % 2, :], func, bias=b1[:, m:m + 1])\
                        .then_inc(f.hid, 1)

        class Chain:

            def __init__(self, eng, s):
                self.eng, self.s, self.n = eng, s, 0

            def __call__(self, ins):
                self.n += 1
                ins.then_inc(self.s, 1)
                self.eng.wait_ge(self.s, self.n)

        def quantise(v, link, x, scr):
            ax, lowc, upc, sc, rs = scr
            xb = x.rearrange("p (b k) -> p b k", k=QB)
            nb = x.shape[1] // QB

            def wide(s):
                return s.unsqueeze(2).to_broadcast([P, nb, QB])

            link(v.tensor_reduce(sc, xb, AX.X, ALU.max, apply_absolute_value=True))
            link(v.tensor_scalar(sc, sc, 1.0 / 6.0, 1e-12, ALU.mult, ALU.max))
            link(v.reciprocal(rs, sc))
            link(v.tensor_tensor(ax.rearrange("p (b k) -> p b k", k=QB), xb, wide(rs), ALU.mult))
            link(v.tensor_scalar(ax.bitcast(I32), ax.bitcast(I32), 2 ** 31 - 1, None, ALU.bitwise_and))
            v.tensor_scalar(upc, ax, GRID_UP[0], 2.0, ALU.is_gt, ALU.mult)
            link(v.tensor_scalar(lowc, ax, GRID_LOW[0], None, ALU.is_gt))
            for k in range(2):
                v.scalar_tensor_tensor(upc, ax, GRID_UP[1 + k], upc, ALU.is_gt, ALU.add)
                link(v.scalar_tensor_tensor(lowc, ax, GRID_LOW[1 + k], lowc, ALU.is_gt, ALU.add))
            link(v.scalar_tensor_tensor(lowc, ax, GRID_LOW[3], lowc, ALU.is_gt, ALU.add))
            link(v.scalar_tensor_tensor(lowc, lowc, 0.5, upc, ALU.mult, ALU.add))
            link(v.scalar_tensor_tensor(ax.bitcast(I32), x.bitcast(I32), -2 ** 31, lowc.bitcast(I32),
                                        ALU.bitwise_and, ALU.bitwise_or))
            link(v.tensor_tensor(xb, ax.rearrange("p (b k) -> p b k", k=QB), wide(sc), ALU.mult))

        QC = TC * FF0
        raw = QS[:, :, :, :].rearrange("p a b c -> p (a b c)").bitcast(F32)
        wn = raw[:, 0:6 * P + FF0]
        wgu = raw[:, 1152:1152 + 2 * FF0]
        wd = raw[:, 1920:1920 + 3 * P]
        hid = raw[:, 2304:2304 + QC]
        hidt = raw[:, 3712:3712 + 3 * CH]
        scr_big = [raw[:, 5248 + QC * i:5248 + QC * (i + 1)] for i in range(2)] + [PB[:, 0, 0:QC]]
        scr_s = [PB[:, 1, 0:160], PB[:, 1, 160:320]]
        silu = PB[:, 1, 512:512 + 2 * FF0].rearrange("p (k n) -> p k n", k=2)
        KT = [P, P, FF0 - 2 * P]

        qn_ready, qw_ready, qh_ready = sem("qn_ready"), sem("qw_ready"), sem("qh_ready")
        wt_filled, wt_ready = sem("wt_filled"), sem("wt_ready")
        f0_ht_filled, f0_ht_ready = sem("f0_ht_filled"), sem("f0_ht_ready")
        gu_filled, gu_silu, gu_done = sem("gu_filled"), sem("gu_silu"), sem("gu_done")
        h0_filled, h0_ready = sem("h0_filled"), sem("h0_ready")
        dn_filled, dn_added = sem("dn_filled"), sem("dn_added")
        w0_in, chain0, chain1, zeroed = sem("w0_in"), sem("chain0"), sem("chain1"), sem("zeroed")
        WT = [(0, c, k) for c in range(2) for k in range(3)] + [(1, 0, k) for k in range(3)]

        def pe_fp4(pe):
            pe.wait_ge(qw_ready, 1)
            pe.wait_ge(A0.res, NC)
            for z, (down, c, k) in enumerate(WT):
                if z >= 2:
                    pe.wait_ge(wt_ready, z - 1)
                rows = KT[k]
                if down:
                    src, m, n = wn[:, 6 * P + P * k:6 * P + P * k + rows], rows, P
                    pe.transpose(pG[0:m, z % 2, 0:P], src, ident[:, :]).then_inc(wt_filled, 1)
                else:
                    src = wn[0:rows, (3 * c + k) * P:(3 * c + k + 1) * P]
                    pe.transpose(pG[:, z % 2, 0:rows], src, ident[0:rows, 0:rows]).then_inc(wt_filled, 1)
            for c in range(NC):
                pe.wait_ge(qn_ready, 1)
                pe.wait_ge(wt_ready, min(len(WT), len(WT) - 1 + c))
                if c >= 2:
                    pe.wait_ge(f0_ht_ready, c - 1)
                z = c + len(WT)
                for i in range(TC):
                    ins = pe.transpose(pG[:, z % 2, i * P:(i + 1) * P], N[:, TC * c + i, :], ident[:, :])
                ins.then_inc(f0_ht_filled, 1)
            pe.wait_ge(f0_ht_ready, NC)
            for c in range(NC):
                for i in range(TC):
                    t = TC * c + i
                    if t > 0:
                        pe.wait_ge(gu_done, t)
                    if i == 0 and c > 0:
                        pe.wait_ge(dn_added, c)
                    for k in range(2):
                        ins = pe.matmul(pG[:, k, 0:FF0], HT[:, t * P:(t + 1) * P], wgu[:, k * FF0:(k + 1) * FF0],
                                        start=True, stop=True)
                    ins.then_inc(gu_filled, 1)
                pe.wait_ge(qh_ready, c + 1)
                for k in range(3):
                    z = 3 * c + k
                    if k >= 2:
                        pe.wait_ge(h0_ready, z - 1)
                    for i in range(TC):
                        ins = pe.transpose(pG[0:KT[k], k % 2, i * P:(i + 1) * P],
                                           hid[:, i * FF0 + k * P:i * FF0 + k * P + KT[k]], ident[:, :])
                    ins.then_inc(h0_filled, 1)
                pe.wait_ge(h0_ready, 3 * c + 3)
                for i in range(TC):
                    for k in range(3):
                        ins = pe.matmul(pG[:, 1, i * P:(i + 1) * P], hidt[0:KT[k], k * CH + i * P:k * CH + (i + 1) * P],
                                        wd[0:KT[k], k * P:(k + 1) * P], start=(k == 0), stop=(k == 2))
                ins.then_inc(dn_filled, 1)

        def act_fp4(act):
            for z, (down, c, k) in enumerate(WT):
                act.wait_ge(wt_filled, z + 1)
                rows = KT[k]
                if down:
                    ins = act.activation(wd[0:rows, P * k:P * (k + 1)], pG[0:rows, z % 2, 0:P], ACT.Identity)
                else:
                    ins = act.activation(wgu[:, c * FF0 + P * k:c * FF0 + P * k + rows], pG[:, z % 2, 0:rows],
                                         ACT.Identity)
                ins.then_inc(wt_ready, 1)
            for c in range(NC):
                act.wait_ge(f0_ht_filled, c + 1)
                act.activation(HT[:, c * CH:(c + 1) * CH], pG[:, (c + len(WT)) % 2, :], ACT.Identity)\
                    .then_inc(f0_ht_ready, 1)
            for c in range(NC):
                for i in range(TC):
                    t = TC * c + i
                    act.wait_ge(gu_filled, t + 1)
                    if t >= 2:
                        act.wait_ge(gu_done, t - 1)
                    act.activation(silu[:, t % 2, :], pG[:, 0, 0:FF0], ACT.Silu).then_inc(gu_silu, 1)
                for k in range(3):
                    act.wait_ge(h0_filled, 3 * c + k + 1)
                    if c >= 1 and k == 0:
                        act.wait_ge(dn_filled, c)
                    act.activation(hidt[0:KT[k], k * CH:(k + 1) * CH], pG[0:KT[k], k % 2, :], ACT.Identity)\
                        .then_inc(h0_ready, 1)

        def dve_fp4(v):
            for c in range(NC):
                ln_stats(v, lnB, X, c)
                if c:
                    ln_norm(v, lnB, X, N, c - 1)
            ln_norm(v, lnB, X, N, NC - 1)
            v.wait_ge(lnB.ready, lnB.off + NC)
            v.wait_ge(zeroed, 2)
            v.wait_ge(w0_in, 96)
            link = Chain(v, chain0)
            quantise(v, link, wn, [s[:, 0:6 * P + FF0] for s in scr_big] + [s[:, 0:(6 * P + FF0) // QB] for s in scr_s])
            v.tensor_copy(mres[:, 0, 0:1], rstd[:, 0:1]).then_inc(qw_ready, 1)
            for half in range(2):
                x = N[:, half * NB:(half + 1) * NB, :].rearrange("p t d -> p (t d)")
                quantise(v, link, x, [s[:, 0:NB * D] for s in scr_big] + [s[:, 0:NB * D // QB] for s in scr_s])
            v.tensor_copy(mres[:, 0, 1:2], rstd[:, 0:1]).then_inc(qn_ready, 1)
            for c in range(NC):
                for i in range(TC):
                    t = TC * c + i
                    v.wait_ge(gu_silu, t + 1)
                    v.tensor_tensor(hid[:, i * FF0:(i + 1) * FF0], silu[:, t % 2, :], pG[:, 1, 0:FF0], ALU.mult)\
                        .then_inc(gu_done, 1)
                v.wait_ge(gu_done, TC * (c + 1))
                quantise(v, link, hid, scr_big + [s[:, 0:QC // QB] for s in scr_s])
                v.tensor_copy(mres[:, 0, 2 + c:3 + c], rstd[:, 0:1]).then_inc(qh_ready, 1)
                v.wait_ge(dn_filled, c + 1)
                ts = slice(TC * c, TC * (c + 1))
                v.tensor_tensor(X[:, ts, :], pG[:, 1, :].rearrange("p (t d) -> p t d", t=TC), X[:, ts, :], ALU.add)\
                    .then_inc(dn_added, 1)

        ln_in = sem("ln_in")
        F1 = Ffn("f1")
        FD = Ffn("fd")
        hb2 = sem("hb2")
        wE_free = sem("wE_free")
        lnf_step = sem("lnf_step")
        out_sem = sem("out_sem")
        c0_in, tail_in, pos_in = sem("c0_in"), sem("tail_in"), sem("pos_in")

        cD = sb("cD", [P, NHID])
        rD = sb("rD", [P, 3, D])

        block = ctx.enter_context(nc.Block())

        @block.sync
        def _(sp):
            sp.dma_start(X[:, :, :], io["x"].rearrange("(t p) d -> p t d", p=P)).then_inc(x_in, 16)
            for dst, src in ((ident[:, :], io["ident"]), (identb[:, :], io["identb"]), (negm[:, :], io["negm"]),
                             (floors[:, :, :], io["floors"])):
                sp.dma_start(dst, src).then_inc(consts_in, 16)
            sp.dma_start(wE[:, :, :], io["w0"][:, 0:3 * D].rearrange("p (a d) -> p a d", a=3)).then_inc(c0_in, 16)
            sp.dma_start(wL[:, 0:D], io["w0"][:, 3 * D:4 * D]).then_inc(c0_in, 16)
            sp.dma_start(rE[:, 0, :], io["b0"].partition_broadcast(P)).then_inc(c0_in, 16)
            sp.wait_ge(made, 1)
            for k in range(RING):
                for h in range(HG):
                    sp.dma_start(KS[R_PAIR:R_B, k, h, :], io["kbits"]).then_inc(consts_in, 16)
            sp_attend(sp, A0, 0)
            sp.wait_ge(A0.b_scored, U * A0.n)
            sp.wait_ge(zeroed, 2)
            for c, name in enumerate(("w_gate", "w_up")):
                sp.dma_start(wn[:, 3 * c * P:(3 * c + 2) * P].rearrange("p (k d) -> p k d", k=2),
                             io[name][0:2 * P, :].rearrange("(k p) d -> p k d", p=P)).then_inc(w0_in, 16)
                sp.dma_start(wn[0:KT[2], (3 * c + 2) * P:(3 * c + 3) * P], io[name][2 * P:FF0, :]).then_inc(w0_in, 16)
            sp.dma_start(wn[:, 6 * P:6 * P + FF0], io["w_down"]).then_inc(w0_in, 16)
            sp.dma_start(cD[:, :], io["cD"]).then_inc(w0_in, 16)
            sp.wait_ge(A0.res, NC)
            sp.dma_start(rD[:, :, :], io["rD"].partition_broadcast(P)).then_inc(tail_in, 16)
            for dst, src in ((wE[:, :, :], io["wE"][0].rearrange("p (a d) -> p a d", a=3)), (cE[:, :], io["cE"][0]),
                             (rE[:, :, :].rearrange("p a d -> p (a d)"), io["rE"][0].partition_broadcast(P))):
                sp.dma_start(dst, src).then_inc(wE_in, 16)
            sp.wait_ge(dn_filled, NC)
            sp.dma_start(pos, io["pos"].rearrange("(t p) d -> p t d", p=P)).then_inc(pos_in, 16)
            sp.wait_ge(made, 2)
            for k in range(RING):
                for h in range(HG):
                    sp.dma_start(QS[R_PAIR:R_A, k, h, :], io["qbits"]).then_inc(mask_in, 16)
            with sp.Fori(0, LAYERS) as layer:
                sp.wait_ge(wE_free, layer * 2 + 1)
                for dst, src in ((wL[:, :], io["wL"]), (cL[:, :], io["cL"])):
                    sp.dma_start(dst, src[bass.ds(layer, 1), :, :].rearrange("o p n -> (o p) n")).then_inc(wL_in, 16)
                sp.dma_start(rL[:, :, :].rearrange("p a d -> p (a d)"),
                             io["rL"][bass.ds(layer, 1), :].rearrange("o n -> (o n)").partition_broadcast(P))\
                    .then_inc(wL_in, 16)
                sp_attend(sp, A1, layer)
                sp.wait_ge(A1.v_evac, layer * NC + NC)
                sp.wait_ge(A1.hb_step, layer * 3 + 3)
                for dst, src in ((wE[:, :, :].rearrange("p a d -> p (a d)"), io["wE"]), (cE[:, :], io["cE"])):
                    sp.dma_start(dst, src[bass.ds(layer + 1, 1), :, :].rearrange("o p n -> (o p) n")).then_inc(wE_in, 16)
                sp.dma_start(rE[:, :, :].rearrange("p a d -> p (a d)"),
                             io["rE"][bass.ds(layer + 1, 1), :].rearrange("o n -> (o n)").partition_broadcast(P))\
                    .then_inc(wE_in, 16)
            sp.wait_ge(wE_free, 2 * LAYERS + 1)
            sp.dma_start(wL[:, D:D + 2 * HID], io["wD"]).then_inc(tail_in, 16)
            for c in range(NC):
                sp.wait_ge(FD.out, c + 1)
                sp.dma_start(io["out"][c * CH:(c + 1) * CH, :].rearrange("(t p) d -> p t d", p=P),
                             X[:, TC * c:TC * (c + 1), :]).then_inc(out_sem, 16)
            sp.wait_ge(out_sem, 16 * NC)

        @block.tensor
        def _(pe):
            pe.wait_ge(consts_in, 16 * (4 + RING * HG))
            pe.wait_ge(c0_in, 48)
            pe_project(pe, A0, lnA.ready, 0, wE[:, 0, :], wE[:, 1, :], wE[:, 2, :])
            pe_attend(pe, A0, 0)
            pe_output(pe, A0, 0, wL[:, 0:D])
            pe_fp4(pe)
            pe.wait_ge(mask_in, 16 * RING * HG)
            with pe.Fori(0, LAYERS) as layer:
                pe.wait_ge(wE_in, layer * 48 + 48)
                pe.wait_ge(wE_free, layer * 2 + 1)
                pe_project(pe, A1, ln_in, layer, wE[:, 0, :], wE[:, 1, :], wE[:, 2, :])
                pe_attend(pe, A1, layer)
                pe_masked(pe, A1, layer)
                pe.wait_ge(wL_in, layer * 48 + 48)
                pe_output(pe, A1, layer, wL[:, 0:D])
                pe_ffn(pe, F1, ln1.ready, 0, layer, wL[:, D:D + HID], wL[:, D + HID:D + 2 * HID], A1.res)
            pe.wait_ge(tail_in, 32)
            pe_ffn(pe, FD, lnD.ready, lnD.off, 0, wL[:, D:D + HID], wL[:, D + HID:D + 2 * HID])

        @block.scalar
        def _(act):
            act_project(act, A0, 0, 1.0, 0.0)
            act_attend(act, A0, 0)
            act_output(act, A0, 0)
            act_fp4(act)
            with act.Fori(0, LAYERS) as layer:
                act.wait_ge(wE_in, layer * 48 + 48)
                act_project(act, A1, layer, cE[:, 2:3], cE[:, 3:4])
                act_attend(act, A1, layer)
                act_output(act, A1, layer)
                act_ffn(act, F1, layer, ACT.Gelu, cL[:, 2:2 + NHID], cL[:, 0:1], cL[:, 1:2])
            act_ffn(act, FD, 0, ACT.Relu, cD[:, :])

        @block.gpsimd
        def _(g):
            def rows(ap, n=NT):
                return ap.unsqueeze(1).to_broadcast([P, n, D])

            g.wait_ge(made, 1)
            for c in range(NC):
                ln_pow(g, lnA, c)
            g.wait_ge(x_in, 16)
            g.wait_ge(c0_in, 48)
            g.tensor_tensor(HB[:, :, :], X[:, :, :], rows(rE[:, 0, :]), ALU.add).then_inc(A0.hb_step, 3)
            for c in range(NC):
                ln_pow(g, lnB, c)
            for c in range(NC):
                ln_pow(g, lnC, c)
            with g.Fori(0, LAYERS) as layer:
                def residual(step, per, gam, bet, bias, ready_all, base):
                    g.tensor_tensor(bet, bet, bias, ALU.add).then_inc(step, 1)
                    g.tensor_tensor(HB[:, :, :], N[:, :, :], rows(gam), ALU.mult).then_inc(step, 1)
                    g.wait_ge(step, layer * 3 + 2)
                    g.tensor_tensor(HB[:, :, :], HB[:, :, :], rows(bet), ALU.add).then_inc(step, 1)

                g.wait_ge(wE_in, layer * 48 + 48)
                g.wait_ge(ln_in, layer * NC + NC)
                g.wait_ge(wE_free, layer * 2 + 1)
                residual(A1.hb_step, 3, rE[:, 0, :], rE[:, 1, :], rE[:, 3, :], None, None)
                g.wait_ge(A1.v_evac, layer * NC + NC)
                for b in range(B):
                    vb = V[:, b * NB * VT:(b + 1) * NB * VT].rearrange("p (x k w) -> p x k w", k=2, w=VT)
                    ub = VU[:, b, :, :]
                    q = ub.rearrange("p (x k) w -> p x k w", k=2)
                    g.tensor_tensor(q[:, :, 1, :], vb[:, :, 1, :], vb[:, :, 0, :], ALU.add).then_inc(A1.u_step, 1)
                    g.tensor_copy(q[:, :, 0, :], vb[:, :, 0, :]).then_inc(A1.u_step, 1)
                    for bit in (1, 2):
                        g.wait_ge(A1.u_step, layer * 4 * B + 4 * b + bit + 1)
                        q = ub.rearrange("p (x k y) w -> p x k (y w)", k=2, y=1 << bit)
                        g.tensor_tensor(q[:, :, 1, :], q[:, :, 1, :], q[:, :, 0, :], ALU.add).then_inc(A1.u_step, 1)
                for c in range(NC):
                    ln_pow(g, ln1, c, layer)
                g.wait_ge(wL_in, layer * 48 + 48)
                g.wait_ge(ln1.ready, layer * NC + NC)
                residual(hb2, 3, rL[:, 0, :], rL[:, 1, :], rL[:, 2, :], None, None)
                for c in range(NC):
                    ln_pow(g, ln2, c, layer)
            for ln in (lnF, lnD):
                for c in range(NC):
                    ln_pow(g, ln, c)

        @block.vector
        def _(v):
            for buf in (QS, KS):
                v.memset(buf[:, :, :, :].rearrange("p a b c -> p (a b c)"), 0.0)
            v.memset(V[:, :], 1.0)
            v.memset(ones[:, :], 1.0)
            v.memset(mhalf[:, :], -0.5).then_inc(made, 1)
            v.wait_ge(x_in, 16)
            for c in range(NC):
                ln_stats(v, lnA, X, c)
                if c:
                    ln_norm(v, lnA, X, N, c - 1)
            ln_norm(v, lnA, X, N, NC - 1)
            dve_project(v, A0, 0, None)
            dve_attend(v, A0, 0)
            v.wait_ge(A0.ht_filled, NC)
            dve_divide(v, A0, 0)
            for c in range(NC):
                ts = slice(TC * c, TC * (c + 1))
                v.wait_ge(A0.wo_filled, c + 1)
                v.wait_ge(A0.hb_step, 3)
                v.tensor_tensor(X[:, ts, :], pG[:, c % 2, :].rearrange("p (t d) -> p t d", t=TC), HB[:, ts, :],
                                ALU.add).then_inc(A0.res, 1)
            v.wait_ge(A0.res, NC)
            v.wait_ge(A0.b_scored, U * A0.n)
            v.memset(wn[:, 2 * P:3 * P], 0.0).then_inc(zeroed, 1)
            v.memset(wn[:, 5 * P:6 * P], 0.0).then_inc(zeroed, 1)
            dve_fp4(v)
            v.wait_ge(dn_added, NC)
            v.memset(QS[:, :, :, :].rearrange("p a b c -> p (a b c)"), 0.0).then_inc(made, 1)
            for c in range(NC):
                ln_stats(v, lnC, X, c)
                if c:
                    ln_norm(v, lnC, X, N, c - 1)
            ln_norm(v, lnC, X, N, NC - 1)
            v.wait_ge(lnC.ready, lnC.off + NC)
            v.wait_ge(pos_in, 16)
            for b in range(B):
                nb = N[:, b * NB:(b + 1) * NB, :]
                v.tensor_tensor(nb, nb, pos, ALU.add).then_inc(ln_in, NC // B)
            v.tensor_copy(mres[:, 0, 6:7], rstd[:, 0:1]).then_inc(wE_free, 1)
            with v.Fori(0, LAYERS) as layer:
                v.wait_ge(wE_in, layer * 48 + 48)
                v.tensor_scalar(bqs[:, :], cE[:, 0:1], SCALE, None, ALU.mult).then_inc(A1.bqs, 1)
                dve_project(v, A1, layer, rE[:, 2, :])
                dve_attend(v, A1, layer)
                dve_masked(v, A1, layer)
                dve_divide(v, A1, layer)
                dve_residual(v, A1, layer, N, ln1)
                for c in range(NC):
                    ts = slice(TC * c, TC * (c + 1))
                    z = FFN.index(("out", c, 0))
                    v.wait_ge(F1.filled, layer * len(FFN) + z + 1)
                    v.wait_ge(hb2, layer * 3 + 3)
                    v.tensor_tensor(N[:, ts, :], pG[:, z % 2, :].rearrange("p (t d) -> p t d", t=TC), HB[:, ts, :],
                                    ALU.add).then_inc(F1.out, 1)
                    v.wait_ge(F1.out, layer * NC + c + 1)
                    ln_stats(v, ln2, N, c, layer, NC)
                    v.wait_ge(ln2.rs, layer * NC + c + 1)
                    for i in range(TC):
                        t = TC * c + i
                        ins = v.tensor_scalar(N[:, t, :], N[:, t, :], mv[:, t, 0:1], rstd[:, t:t + 1],
                                              ALU.subtract, ALU.mult)
                    ins.then_inc(ln_in, 1)
                v.tensor_copy(mres[:, 0, 7:8], rstd[:, 0:1]).then_inc(wE_free, 2)
            link = Chain(v, lnf_step)
            v.wait_ge(wE_in, 48 * (LAYERS + 1))
            v.wait_ge(ln_in, NC * (LAYERS + 1))

            def row(ap):
                return ap.unsqueeze(1).to_broadcast([P, NT, D])

            link(v.tensor_tensor(N[:, :, :], N[:, :, :], row(rE[:, 0, :]), ALU.mult))
            link(v.tensor_tensor(N[:, :, :], N[:, :, :], row(rE[:, 1, :]), ALU.add))
            for c in range(NC):
                ln_stats(v, lnF, N, c)
                if c:
                    ln_norm(v, lnF, N, N, c - 1)
            ln_norm(v, lnF, N, N, NC - 1)
            v.wait_ge(lnF.ready, lnF.off + NC)
            v.wait_ge(tail_in, 16)
            link(v.tensor_tensor(N[:, :, :], N[:, :, :], row(rD[:, 0, :]), ALU.mult))
            link(v.tensor_tensor(N[:, :, :], N[:, :, :], row(rD[:, 1, :]), ALU.add))
            link(v.tensor_tensor(X[:, :, :], X[:, :, :], N[:, :, :], ALU.add))
            for c in range(NC):
                ln_stats(v, lnD, X, c)
                if c:
                    ln_norm(v, lnD, X, N, c - 1)
            ln_norm(v, lnD, X, N, NC - 1)
            v.wait_ge(lnD.ready, lnD.off + NC)
            link(v.tensor_tensor(X[:, :, :], X[:, :, :], row(rD[:, 2, :]), ALU.add))
            for c in range(NC):
                ts = slice(TC * c, TC * (c + 1))
                z = FFN.index(("out", c, 0))
                v.wait_ge(FD.filled, z + 1)
                v.tensor_tensor(X[:, ts, :], pG[:, z % 2, :].rearrange("p (t d) -> p t d", t=TC), X[:, ts, :],
                                ALU.add).then_inc(FD.out, 1)


def kernel(**inputs):
    import numpy as np
    import concourse.bacc as bacc
    from concourse.bass_utils import run_bass_kernel_spmd as run

    f32 = np.float32
    g = {k: np.ascontiguousarray(v) for k, v in inputs.items()}
    import ml_dtypes
    bf = ml_dtypes.bfloat16

    def dh(w):
        return w.reshape(w.shape[:-1] + (H, HD)).swapaxes(-1, -2).reshape(w.shape)

    at = np.arange(S)
    bits = ((at[None, :] >> np.arange(NBIT)[:, None]) & 1).astype(f32)
    low = np.arange(P)
    negm = -((low[:, None] & low[None, :]) == 0).astype(f32)
    big = f32(2.0 ** 60)
    floors = np.zeros((P, 2, NB), f32)
    floors[0, 0, 0], floors[0, 1, 0] = -big, big
    level = np.frexp((at + 1).astype(np.float64))[1] - 1
    coord = (at >> level) / 2.0 ** level
    div = np.exp(np.arange(0, D, 2, dtype=np.float64) * -(np.log(10000.0) / D))
    ang = at[:, None].astype(np.float64) * div[None, :]
    pos = np.zeros((S, D), f32)
    pos[:, 0::2] = (np.sin(ang) * coord[:, None]).astype(f32)
    pos[:, 1::2] = (np.cos(ang) * coord[:, None]).astype(f32)

    w0 = g["L0_attn_w_qkv"]
    one, zero = np.ones((1, D), f32), np.zeros((1, D), f32)
    gin = np.concatenate([one, g["L1_attn_ln2_g"]])
    bin_ = np.concatenate([zero, g["L1_attn_ln2_b"]])

    def pad(w):
        return np.concatenate([w, w[:1]])

    def cols(*ws):
        return np.ascontiguousarray(np.stack(ws, -1))

    arrays = {
        "x": g["L0_attn_x"].reshape(B * S, D),
        "ident": np.eye(P, dtype=f32), "identb": np.eye(P, dtype=f32).astype(bf),
        "negm": negm, "floors": floors, "pos": pos,
        "kbits": np.concatenate([bits, np.ones((NP, S), f32)]).astype(bf),
        "qbits": (-big * bits).astype(bf),
        "w0": np.concatenate([dh(w0[:, 0:D]), dh(w0[:, D:2 * D]), w0[:, 2 * D:], g["L0_attn_w_proj"]], 1),
        "b0": g["L0_attn_b_proj"],
        "w_gate": g["L0_ffn_w_gate"], "w_up": g["L0_ffn_w_up"], "w_down": g["L0_ffn_w_down"],
        "wE": pad(np.concatenate([dh(g["L1_attn_Wq"]), dh(g["L1_attn_Wk"]), g["L1_attn_Wv"]], 2)),
        "cE": cols(pad(dh(g["L1_attn_bq"])), pad(dh(g["L1_attn_bk"])), gin, bin_),
        "rE": np.concatenate([gin, bin_, pad(g["L1_attn_bv"]), pad(g["L1_attn_bo"])], 1),
        "wL": np.concatenate([g["L1_attn_Wo"], g["L1_attn_W1"],
                              g["L1_attn_W2"].reshape(LAYERS, NHID, P, D).swapaxes(1, 2).reshape(LAYERS, P, HID)], 2),
        "cL": np.concatenate([cols(g["L1_attn_ln1_g"], g["L1_attn_ln1_b"]),
                              g["L1_attn_b1"].reshape(LAYERS, NHID, P).swapaxes(1, 2)], 2),
        "rL": np.concatenate([g["L1_attn_ln1_g"], g["L1_attn_ln1_b"], g["L1_attn_b2"]], 1),
        "wD": np.concatenate([g["L1_ffn_W1"], g["L1_ffn_W2"].reshape(NHID, P, D).swapaxes(0, 1).reshape(P, HID)], 1),
        "cD": g["L1_ffn_b1"].reshape(NHID, P).T,
        "rD": np.concatenate([g["L1_attn_lnf_g"], g["L1_attn_lnf_b"], g["L1_ffn_b2"]]),
    }
    arrays = {k: np.ascontiguousarray(v) for k, v in arrays.items()}
    nc = bacc.Bacc("TRN2", target_bir_lowering=False, num_devices=1)
    io = {k: nc.dram_tensor("in_" + k, v.shape, mybir.dt.from_np(v.dtype), kind="ExternalInput").ap()
          for k, v in arrays.items()}
    io["out"] = nc.dram_tensor("out", (B * S, D), F32, kind="ExternalOutput").ap()
    nc.disable_value_cache = True
    build(nc, io)
    r = run(nc, [{"in_" + k: v for k, v in arrays.items()}], core_ids=[0])
    return r.results[0]["out"].reshape(B, S, D)
```
